# Optimizing a Trainium2 kernel written in Bass

```python
import numpy as np
import jax
import jax.numpy as jnp

def _softmax(x, axis=-1):
    return jax.nn.softmax(x, axis=axis)

def _gelu(x):
    return jax.nn.gelu(x, approximate=True)

def _silu(x):
    return jax.nn.silu(x)

def _sigmoid(x):
    return jax.nn.sigmoid(x)

def _layernorm(x, axis=-1, eps=1e-05):
    m = jnp.mean(x, axis=axis, keepdims=True)
    v = jnp.var(x, axis=axis, keepdims=True)
    return (x - m) / jnp.sqrt(v + eps)

def _scatter_add(tgt, idx, src, axis=0):
    return tgt.at[idx].add(src)

def _segment_sum(src, seg, n):
    return jax.ops.segment_sum(src, seg, n)
kernel_name = 'mk_adaln_d1_jaxref_r8_816e53'

def setup_inputs(seed: int=0):
    np.random.seed(seed)
    _w = jnp.asarray

    def _L0_attn_setup():
        import jax, jax.numpy as jnp
        import numpy as np
        D_MODEL, D_K, D_V, N_HEADS = (128, 64, 64, 16)
        B, T = (4, 256)

        def _xavier(key, shape, gain):
            fan_in, fan_out = (shape[0], shape[1])
            a = gain * np.sqrt(6.0 / (fan_in + fan_out))
            return jax.random.uniform(key, shape, jnp.float32, -a, a)
        key = jax.random.key(seed)
        ks = jax.random.split(key, 6)
        H, dk, dv, d = (N_HEADS, D_K, D_V, D_MODEL)
        return {'x': jax.random.normal(ks[0], (B, T, d), jnp.float32), 'W_q': _xavier(ks[1], (d, H * dk), 0.1), 'W_k': _xavier(ks[2], (d, H * dk), 0.1), 'W_v': _xavier(ks[3], (d, H * dv), 0.1), 'W_gate': _xavier(ks[4], (d, H * dk), 0.01), 'b_gate': jnp.full((H * dk,), 3.0, jnp.float32), 'W_o': _xavier(ks[5], (H * dv, d), 0.1)}
    _L0_attn_in = _L0_attn_setup()

    def _L0_ffn_setup():
        import jax, jax.numpy as jnp
        import numpy as np
        B, S, H = (2, 256, 128)
        E_ROUTED = 8
        TOP_K = 2
        I = 256
        key = jax.random.key(seed)
        ks = jax.random.split(key, 9)
        s = 0.02
        return {'x': jax.random.normal(ks[0], (B, S, H), dtype=jnp.float32), 'shared_gate': jax.random.normal(ks[1], (I, H), dtype=jnp.float32) * s, 'shared_up': jax.random.normal(ks[2], (I, H), dtype=jnp.float32) * s, 'shared_down': jax.random.normal(ks[3], (H, I), dtype=jnp.float32) * s, 'gate_w': jax.random.normal(ks[4], (E_ROUTED, H, I), dtype=jnp.float32) * s, 'up_w': jax.random.normal(ks[5], (E_ROUTED, H, I), dtype=jnp.float32) * s, 'down_w': jax.random.normal(ks[6], (E_ROUTED, I, H), dtype=jnp.float32) * s, 'router_w': jax.random.normal(ks[7], (E_ROUTED, H), dtype=jnp.float32) * s, 'routing_bias': jnp.zeros((E_ROUTED,), dtype=jnp.float32)}
    _L0_ffn_in = _L0_ffn_setup()
    _L0_c = _w((lambda *s: np.random.randn(*s).astype(np.float32) * 0.05)(32, 128))
    _L0_wmod = _w((lambda *s: np.random.randn(*s).astype(np.float32) * 0.05)(128, 6 * 128) * 128 ** (-0.5))
    _d = {'L0_attn_x': _L0_attn_in['x'], 'L0_attn_W_q': _L0_attn_in['W_q'], 'L0_attn_W_k': _L0_attn_in['W_k'], 'L0_attn_W_v': _L0_attn_in['W_v'], 'L0_attn_W_gate': _L0_attn_in['W_gate'], 'L0_attn_b_gate': _L0_attn_in['b_gate'], 'L0_attn_W_o': _L0_attn_in['W_o'], 'L0_ffn_shared_gate': _L0_ffn_in['shared_gate'], 'L0_ffn_shared_up': _L0_ffn_in['shared_up'], 'L0_ffn_shared_down': _L0_ffn_in['shared_down'], 'L0_ffn_gate_w': _L0_ffn_in['gate_w'], 'L0_ffn_up_w': _L0_ffn_in['up_w'], 'L0_ffn_down_w': _L0_ffn_in['down_w'], 'L0_ffn_router_w': _L0_ffn_in['router_w'], 'L0_ffn_routing_bias': _L0_ffn_in['routing_bias'], 'L0_c': _L0_c, 'L0_wmod': _L0_wmod}
    _x0 = _d['L0_attn_x']
    _d['L0_attn_x'] = jax.random.normal(jax.random.fold_in(jax.random.key(seed), 1), (32, 256, 128), dtype=_x0.dtype)
    del _x0
    return _d

def reference(L0_attn_x, L0_attn_W_q, L0_attn_W_k, L0_attn_W_v, L0_attn_W_gate, L0_attn_b_gate, L0_attn_W_o, L0_ffn_shared_gate, L0_ffn_shared_up, L0_ffn_shared_down, L0_ffn_gate_w, L0_ffn_up_w, L0_ffn_down_w, L0_ffn_router_w, L0_ffn_routing_bias, L0_c, L0_wmod):

    def _L0_attn_ref(x, W_q, W_k, W_v, W_gate, b_gate, W_o):
        import jax, jax.numpy as jnp
        import numpy as np
        D_MODEL, D_K, D_V, N_HEADS = (128, 64, 64, 16)
        B, T = (4, 256)

        def _xavier(key, shape, gain):
            fan_in, fan_out = (shape[0], shape[1])
            a = gain * np.sqrt(6.0 / (fan_in + fan_out))
            return jax.random.uniform(key, shape, jnp.float32, -a, a)
        Bn, Tn, d = x.shape
        H, dk, dv = (N_HEADS, D_K, D_V)
        q = (x @ W_q).reshape(Bn, Tn, H, dk)
        k = (x @ W_k).reshape(Bn, Tn, H, dk)
        v = (x @ W_v).reshape(Bn, Tn, H, dv)
        a = jax.nn.sigmoid(x @ W_gate + b_gate).reshape(Bn, Tn, H, dk)

        def step(S, qkva):
            q_t, k_t, v_t, a_t = qkva
            S = a_t[..., None] * S + k_t[..., None] * v_t[..., None, :]
            o_t = jnp.einsum('bhk,bhkv->bhv', q_t, S)
            return (S, o_t)
        S0 = jnp.zeros((Bn, H, dk, dv), x.dtype)
        qs = jnp.moveaxis(q, 1, 0)
        ks_ = jnp.moveaxis(k, 1, 0)
        vs = jnp.moveaxis(v, 1, 0)
        as_ = jnp.moveaxis(a, 1, 0)
        _, outs = jax.lax.scan(step, S0, (qs, ks_, vs, as_))
        out = jnp.moveaxis(outs, 0, 1).reshape(Bn, Tn, H * dv)
        return out @ W_o

    def _L0_ffn_ref(x, shared_gate, shared_up, shared_down, gate_w, up_w, down_w, router_w, routing_bias):
        import jax, jax.numpy as jnp
        import numpy as np
        B, S, H = (2, 256, 128)
        E_ROUTED = 8
        TOP_K = 2
        I = 256
        b, s, h = x.shape
        shared = jnp.einsum('bsi,hi->bsh', jax.nn.silu(jnp.einsum('bsh,ih->bsi', x, shared_gate)) * jnp.einsum('bsh,ih->bsi', x, shared_up), shared_down)
        logits = jnp.einsum('bsh,eh->bse', x, router_w) + routing_bias
        probs = jax.nn.sigmoid(logits)
        scores, indices = jax.lax.top_k(probs, TOP_K)
        scores = scores / jnp.sum(scores, axis=-1, keepdims=True)
        t = b * s
        xf = x.reshape(t, h)
        idx = indices.reshape(t, TOP_K)
        sc = scores.reshape(t, TOP_K)
        w = jnp.zeros((t, E_ROUTED), dtype=x.dtype)
        w = w.at[jnp.arange(t)[:, None], idx].add(sc)
        g = jax.nn.silu(jnp.einsum('th,ehi->tei', xf, gate_w))
        u = jnp.einsum('th,ehi->tei', xf, up_w)
        combined = jnp.einsum('tei,eih,te->th', g * u, down_w, w)
        return shared + combined.reshape(b, s, h)
    x = L0_attn_x
    mod = (_silu(L0_c) @ L0_wmod).reshape(L0_c.shape[0], 6, 1, -1)
    sa, ca, ga, sb, cb, gb = (mod[:, 0], mod[:, 1], mod[:, 2], mod[:, 3], mod[:, 4], mod[:, 5])
    ga = (2 * (ga >= 0) - 1) * jnp.maximum(jnp.abs(ga), 0.25)
    gb = (2 * (gb >= 0) - 1) * jnp.maximum(jnp.abs(gb), 0.25)
    h = _layernorm(x, axis=-1) * (1 + ca) + sa
    x = x + ga * _L0_attn_ref(h, L0_attn_W_q, L0_attn_W_k, L0_attn_W_v, L0_attn_W_gate, L0_attn_b_gate, L0_attn_W_o)
    h = _layernorm(x, axis=-1) * (1 + cb) + sb
    x = x + gb * _L0_ffn_ref(h, L0_ffn_shared_gate, L0_ffn_shared_up, L0_ffn_shared_down, L0_ffn_gate_w, L0_ffn_up_w, L0_ffn_down_w, L0_ffn_router_w, L0_ffn_routing_bias)
    return x

_drawn_inputs = setup_inputs


def setup_inputs(seed=0):
    import zlib

    import numpy as np

    out = dict(_drawn_inputs(seed))
    spreads = {'L0_attn_b_gate': (3.0, 0.6), 'L0_ffn_routing_bias': (0.0, 0.8)}
    factors = {'L0_attn_W_q': 8.0,
     'L0_attn_W_k': 8.0,
     'L0_attn_W_v': 8.0,
     'L0_attn_W_gate': 35.54,
     'L0_attn_W_o': 8.0,
     'L0_ffn_shared_gate': 8.0,
     'L0_ffn_shared_up': 8.0,
     'L0_ffn_shared_down': 8.0,
     'L0_ffn_gate_w': 8.0,
     'L0_ffn_up_w': 8.0,
     'L0_ffn_down_w': 8.0,
     'L0_ffn_router_w': 8.0,
     'L0_c': 8.0,
     'L0_wmod': 8.0}
    for name, (base, spread) in spreads.items():
        noise = np.random.default_rng([zlib.crc32(name.encode()), seed]).standard_normal(out[name].shape)
        drawn = base * np.exp(spread * noise) if base else spread * noise
        out[name] = jnp.asarray(drawn.astype(out[name].dtype))
    for name, factor in factors.items():
        out[name] = (out[name] * factor).astype(out[name].dtype)
    return out
```

```python
import math

import concourse.bass as bass
from concourse import mybir
from contextlib import ExitStack

B, T, D = 32, 256, 128
HEADS, DK = 16, 64
P = 128
PAIRS = HEADS * DK // P
CHUNKS = T // P
TILES = B * T // P
E, TOP = 8, 2
I = 256
IT = I // P
NE = E + 1
STEP = 512
ST = STEP // P
STEPS = B * T // STEP
SLICE = E * 2 * I // B
EPS = 1e-5
GATE_FLOOR = 0.25
W_ORDER = (2, 0, 1, 3)
GROWTH_MAX = 1e30
GROWTH_CAP = 1e31


def block_kernel(nc, x, W_q, W_k, W_v, W_gate, b_gate, W_o, shared_gate, shared_up, shared_down,
                 gate_w, up_w, down_w, router_w, routing_bias, c, wmod, out):
    f32, f32r, i32, u32 = mybir.dt.float32, mybir.dt.float32r, mybir.dt.int32, mybir.dt.uint32
    ALU, ACT = mybir.AluOpType, mybir.ActivationFunctionType
    ds = bass.ds

    x_tiles = x.rearrange("b (c p) d -> p (b c) d", p=P)
    out_tiles = out.rearrange("b (c p) d -> p (b c) d", p=P)

    ctx = ExitStack()
    with ctx:
        def sb(name, shape, dt=f32):
            return ctx.enter_context(nc.sbuf_tensor(name, shape, dt))

        def sem(name):
            return ctx.enter_context(nc.semaphore(name))

        gate_rows_dram = nc.dram_tensor("gate_rows_dram", [B, 2, D], f32, kind="Internal").ap()

        xs = sb("xs", [P, TILES, D])
        w_hi = sb("w_hi", [P, 4, HEADS * DK], f32r)
        w_lo = sb("w_lo", [P, 4, HEADS * DK], f32r)
        gu_hi = sb("gu_hi", [P, NE, 2, I], f32r)
        gu_lo = sb("gu_lo", [P, NE, 2, I], f32r)
        down = sb("down", [P, NE, IT, D])
        wo = sb("wo", [P, PAIRS, D])
        ga_all = sb("ga_all", [P, B, D])
        gb_all = sb("gb_all", [P, B, D])
        ident = sb("ident", [P, P])
        cap = sb("cap", [P, P])
        causal = sb("causal", [P, P])
        mod = sb("mod", [P, 4, B])
        half_bg = sb("half_bg", [P, PAIRS])
        neg_bg = sb("neg_bg", [P, PAIRS])
        bgT = sb("bgT", [P, PAIRS])
        rwT = sb("rwT", [P, E])
        rbias = sb("rbias", [P, E])
        iota8 = sb("iota8", [P, E])

        c_in = sb("c_in", [B, D])
        c_e = sb("c_e", [B, D])
        c_s = sb("c_s", [B, D])
        cT = sb("cT", [P, B])
        grow = sb("grow", [B, 2, D])
        gsign = sb("gsign", [B, 2, D])
        rows8 = sb("rows8", [E, 2, P])

        shared = sb("shared", [P, 4608])
        w_in = shared[:, 0:4 * HEADS * DK].rearrange("p (m n) -> p m n", m=4)
        shared_gu_in = shared[:, 4096:4608]
        gu_in = gb_all[:, :, :].rearrange("p b d -> p (b d)")
        v_sb = shared[:, 0:2048].rearrange("p (c n) -> p c n", c=CHUNKS)
        oT = shared[:, 2048:4096].rearrange("p (g t) -> p g t", g=PAIRS)
        act = shared[:, 0:2048].rearrange("p (e i t) -> p e i t", e=2, i=IT)
        silu = shared[:, 2048:3072].rearrange("p (i t) -> p i t", i=IT)
        acc = shared[:, 3072:3584].rearrange("p (n d) -> p n d", n=ST)
        part = shared[:, 3584:4608].rearrange("p (k n d) -> p k n d", k=2, n=ST)

        xn = sb("xn", [P, ST, D])
        stats = sb("stats", [P, ST, 6])
        mv = sb("mv", [P, ST, 2])
        veps = sb("veps", [P, ST])
        rstd = sb("rstd", [P, ST])
        neg_half = sb("neg_half", [P, ST])
        h_full = sb("h_full", [P, STEP])
        h_hi = sb("h_hi", [P, STEP], f32r)
        h_lo = sb("h_lo", [P, STEP], f32r)

        th = sb("th", [P, 2, T])
        ex = sb("ex", [P, 2, T])
        ga_t = sb("ga_t", [P, 2, T])
        gi_t = sb("gi_t", [P, 2, T])
        F = sb("F", [P, 2, T])
        G = sb("G", [P, 2, T])
        kt = sb("kt", [P, 2, T])
        qz = sb("qz", [P, 2, CHUNKS, 2, P])
        kx = sb("kx", [P, 2, P])
        A = sb("A", [P, 2, 2, 3, P])
        y_sb = sb("y_sb", [P, CHUNKS, D])
        grown = sb("grown", [P, 2])

        lg = sb("lg", [P, ST, E])
        inv_e = sb("inv_e", [P, ST, E])
        lg_e = sb("lg_e", [P, ST, E])
        lg_1 = sb("lg_1", [P, ST, E])
        pr = sb("pr", [P, ST, E])
        top = sb("top", [P, ST, 8])
        top_i = sb("top_i", [P, ST, 8], u32)
        top_f = sb("top_f", [P, ST, TOP])
        tsum = sb("tsum", [P, ST])
        trec = sb("trec", [P, ST])
        score = sb("score", [P, ST, TOP])
        pick = sb("pick", [P, TOP, ST, E])
        wts = sb("wts", [P, ST, E])

        seq = lambda first, width: shared[:, first:first + width]
        wst = seq(0, 512).rearrange("p (m n) -> p m n", m=4)
        seq_qk, seq_a, seq_v = seq(512, 512), seq(1024, 256), seq(1280, 256)
        seq_kv, seq_S, seq_qS = seq(1536, 256), seq(1792, 256), seq(2048, 256)
        seq_o = seq(2304, 2048).rearrange("p (g t) -> p g t", g=PAIRS)
        spread, place = seq(4352, P), seq(4480, P)
        table = sb("table", [P, 1])
        flag_p = sb("flag_p", [P, 1])
        ones = sb("ones", [P, 1])
        flag = sb("flag", [1, 1], i32)
        reverse = sb("reverse", [P, P])
        band = sb("band", [P, P + DK])

        banks = [ctx.enter_context(nc.psum_tensor(f"bank{n}", [P, 512], f32)) for n in range(8)]
        QK, Z, SD, SX, O, M = banks[0:2], banks[2], banks[3:5], banks[5], banks[6], banks[7]
        V = M
        Y = SX
        GU, DN, M2, R = [banks[0:2], banks[2:4]], banks[4:6], banks[6], banks[7]

        s_c, s_wmod, s_rows, s_x, s_sh_in, s_misc, s_gu_in = (sem(n) for n in (
            "c_loaded", "wmod_loaded", "rows_loaded", "x_loaded", "shared_expert_loaded", "misc_loaded", "gu_loaded"))
        s_x_next, s_x_rest = sem("x_next_loaded"), sem("x_rest_loaded")
        s_ident, s_const = sem("ident_ready"), sem("consts_ready")
        s_ce, s_cs, s_cT_ps, s_cT = sem("c_exp"), sem("c_silu"), sem("cT_psum"), sem("cT_ready")
        s_mod_ps, s_mod = sem("mod_psum"), sem("mod_ready")
        s_grow_ps, s_grow, s_grow_out = sem("grow_psum"), sem("grow_ready"), sem("grow_stored")
        s_ga, s_gb, s_wo = sem("ga_loaded"), sem("gb_loaded"), sem("wo_loaded")
        s_rows_ps, s_rowsT = sem("rows_psum"), sem("rowsT_ready")
        s_sh_ps, s_sh = sem("shared_psum"), sem("shared_copied")
        s_w_in = [sem("w_loaded_" + n) for n in ("q", "k", "gate", "v")]
        s_whi, s_wsplit, s_guhi, s_gusplit = sem("w_high"), sem("w_split"), sem("gu_high"), sem("gu_split")
        s_veps = sem("variance_eps")
        s_st, s_hh, s_gm, s_rt = (sem(n) for n in (
            "stats_ready", "h_high", "growth_seen", "routing_step"))
        s_dve = sem("vector_step")
        s_pool = sem("pool_step")
        s_mv, s_rs, s_xn, s_T, s_hf, s_hl = (sem(n) for n in (
            "moments_ready", "rstd_ready", "xn_ready", "xT_psum", "h_ready", "h_split"))
        s_z, s_qk, s_te, s_a, s_kt, s_qt, s_kx = (sem(n) for n in (
            "z_psum", "qk_psum", "tanh_exp", "gates_ready", "k_scaled", "q_scaled", "k_across"))
        s_sd, s_sx, s_am, s_ax, s_av, s_o = (sem(n) for n in (
            "diag_psum", "across_psum", "diag_masked", "across_copied", "o_psum", "o_copied"))
        s_vp, s_v, s_y, s_ys, s_xu = (sem(n) for n in (
            "v_psum", "v_copied", "y_psum", "y_copied", "x_updated"))
        s_fg, s_th, s_at = sem("products_scanned"), sem("tanh_ready"), sem("gate_ready")
        s_xn2, s_mv2, s_rs2, s_T2, s_hf2, s_hl2 = (sem(n) for n in (
            "xn2_ready", "moments2_ready", "rstd2_ready", "xT2_psum", "h2_ready", "h2_split"))
        s_r, s_lg, s_le, s_wt = sem("router_psum"), sem("logits_ready"), sem("logits_exp"), sem("weights_ready")
        s_g, s_u, s_silu, s_act = sem("gate_psum"), sem("up_psum"), sem("silu_ready"), sem("act_ready")
        s_dn, s_cb, s_add, s_fin, s_out = (sem(n) for n in (
            "down_psum", "down_scaled", "expert_added", "x_final", "out_stored"))

        s_gflag, s_fps, s_flag = sem("growth_flag"), sem("flag_psum"), sem("flag_ready")
        (s_xr, s_fc, s_fz, s_fst, s_fmv, s_fve, s_frs, s_fxn, s_fT, s_fh, s_fw, s_fp, s_fa, s_fq, s_fs, s_fb,
         s_fcl, s_fv, s_fqs, s_fo, s_fot, s_fy, s_fyg, s_fx) = (sem("seq_" + n) for n in (
            "x_reloaded", "selectors", "zeros", "stats", "moments", "variance_eps", "rstd", "xn", "xT_psum", "h",
            "weights", "projected", "tanh", "inputs", "selected", "v_spread", "o_closed", "step", "q_times_S", "o_added",
            "o_copied", "y_psum", "y_gated", "x_updated"))

        def growing(eng):
            eng.wait_ge(s_flag, 1)
            return eng.If(eng.value_load(flag[0:1, 0:1], min_val=0, max_val=1) > 0)

        def not_growing(eng):
            return eng.If(eng.value_load(flag[0:1, 0:1], min_val=0, max_val=1) < 1)

        block = ctx.enter_context(nc.Block())

        @block.sync
        def _(sp):
            sp.dma_start(c_in[:, :], c).then_inc(s_c, 16)
            sp.dma_start(xs[:, 0:2, :], x_tiles[:, 0:2, :]).then_inc(s_x, 16)
            sp.dma_start(gb_all[:, 0:6, :].rearrange("p b d -> p (b d)"), wmod).then_inc(s_wmod, 16)
            for m, w in ((2, W_gate), (0, W_q)):
                sp.dma_start(w_in[:, m, :], w).then_inc(s_w_in[m], 16)
            sp.dma_start(rows8[:, 0, :], b_gate.rearrange("(g p) -> g p", p=P)).then_inc(s_rows, 16)
            sp.dma_start(rows8[:, 1, :], router_w).then_inc(s_rows, 16)
            for m, w in ((1, W_k), (3, W_v)):
                sp.dma_start(w_in[:, m, :], w).then_inc(s_w_in[m], 16)
            sp.dma_start(xs[:, 2:4, :], x_tiles[:, 2:4, :]).then_inc(s_x_next, 16)
            sp.dma_start(ga_all[:, 0:2, :], shared_gate.rearrange("(i p) h -> p i h", p=P)).then_inc(s_sh_in, 16)
            sp.dma_start(ga_all[:, 2:4, :], shared_up.rearrange("(i p) h -> p i h", p=P)).then_inc(s_sh_in, 16)
            sp.dma_start(ga_all[:, 4:6, :].rearrange("p i h -> p (i h)"), shared_down).then_inc(s_sh_in, 16)
            sp.dma_start(wo[:, :, :], W_o.rearrange("(g p) d -> p g d", p=P)).then_inc(s_wo, 16)
            sp.dma_start(xs[:, 4:TILES, :], x_tiles[:, 4:TILES, :]).then_inc(s_x_rest, 16)
            sp.wait_ge(s_grow, 1)
            sp.dma_start(gate_rows_dram, grow[:, :, :]).then_inc(s_grow_out, 16)
            sp.wait_ge(s_grow_out, 16)
            sp.wait_ge(s_sh_ps, 3)
            def load_gates(k, gates, signal):
                rows = gate_rows_dram[:, k, :].rearrange("(a b) d -> a b d", a=1)
                sp.dma_start(gates[:, :, :], rows.broadcast_to([P, B, D])).then_inc(signal, 16)

            load_gates(0, ga_all, s_ga)
            stage = gu_in.rearrange("p (e m n) -> p e m n", e=E, m=2)
            sp.wait_ge(s_grow_ps, 1)
            sp.dma_start(stage[:, :, 0, :], gate_w.rearrange("e h i -> h e i")).then_inc(s_gu_in, 16)
            sp.dma_start(stage[:, :, 1, :], up_w.rearrange("e h i -> h e i")).then_inc(s_gu_in, 16)
            sp.dma_start(down[:, 1:NE, :, :].rearrange("p e i d -> p (e i) d"),
                         down_w.rearrange("e (i p) d -> p (e i) d", p=P)).then_inc(s_misc, 16)
            sp.dma_start(rbias[:, :], routing_bias.rearrange("(a e) -> a e", a=1).broadcast_to([P, E])).then_inc(s_misc, 16)
            sp.wait_ge(s_gusplit, B)
            load_gates(1, gb_all, s_gb)
            with growing(sp):
                sp.wait_ge(s_xu, B + 1)
                sp.dma_start(xs[:, :, :], x_tiles).then_inc(s_xr, 16)
            with sp.Fori(0, STEPS) as j:
                sp.wait_ge(s_fin, j + 2)
                sp.dma_start(out_tiles[:, ds(j * ST, ST), :], xs[:, ds(j * ST, ST), :]).then_inc(s_out, 16)
            sp.wait_ge(s_out, 16 * STEPS)

        @block.gpsimd
        def _(pool):
            g = nc.gpsimd
            for credited in (s_sx, s_ys, s_am, s_ax, s_o, s_xu, s_fin, s_cb, s_add, s_fo):
                pool.sem_inc(credited, 1)
            g.memset(ident[:, :], 0.0).then_inc(s_pool, 1)
            g.memset(causal[:, :], 1.0).then_inc(s_pool, 1)
            pool.wait_ge(s_pool, 2)
            g.affine_select(out=ident[:, :], in_=ident[:, :], compare_op=ALU.not_equal, fill=1.0,
                            base=0, pattern=[[-1, P]], channel_multiplier=1).then_inc(s_ident, 1)
            g.affine_select(out=causal[:, :], in_=causal[:, :], compare_op=ALU.is_ge, fill=0.0,
                            base=0, pattern=[[1, P]], channel_multiplier=-1).then_inc(s_const, 1)
            g.iota(iota8[:, :], pattern=[[1, E]], base=0, channel_multiplier=0,
                   allow_small_or_imprecise_dtypes=True).then_inc(s_const, 1)
            g.memset(qz[:, :, :, :, :], 0.0).then_inc(s_const, 1)
            g.memset(A[:, :, :, :, :], 0.0).then_inc(s_const, 1)
            g.memset(neg_half[:, :], -0.5).then_inc(s_pool, 1)
            g.memset(ones[:, :], 1.0).then_inc(s_pool, 1)
            g.memset(inv_e[:, :, :], math.exp(-1.0)).then_inc(s_pool, 1)
            g.memset(cap[:, :], GROWTH_CAP).then_inc(s_const, 1)
            g.memset(grown[:, :], 0.0).then_inc(s_const, 1)
            pool.wait_ge(s_pool, 5)

            def alone(semaphore, count):
                count = count if isinstance(count, int) else pool.to_reg(count)
                pool.wait_ge(s_ident, 1)
                pool.wait_ge(semaphore, count)

            def inverse_std(moments, n_tiles, count, signal):
                alone(moments, count)
                g.tensor_scalar(veps[:, 0:n_tiles], mv[:, 0:n_tiles, 1], EPS, None, ALU.add).then_inc(s_veps, 1)
                pool.wait_ge(s_veps, count if moments is s_mv else count + B)
                g.tensor_tensor(rstd[:, 0:n_tiles], veps[:, 0:n_tiles], neg_half[:, 0:n_tiles], ALU.pow).then_inc(signal, 1)

            def gates(n, par):
                alone(s_th, n)
                g.tensor_scalar(ga_t[:, par, :], th[:, par, :], 0.5, 0.5, ALU.mult, ALU.add).then_inc(s_at, 1)
                alone(s_te, n)
                g.tensor_scalar(gi_t[:, par, :], ex[:, par, :], 1.0, 1.0, ALU.mult, ALU.add).then_inc(s_a, 1)

            def body(b, last):
                for p in range(1, PAIRS + 1):
                    if not (last and p >= PAIRS - 1):
                        gates(b * PAIRS + p + 2, (p + 1) % 2)
                    if p == 2 and not last:
                        inverse_std(s_mv, CHUNKS, b + 2, s_rs)
                if not last:
                    update_x(b)

            def update_x(b):
                pool.wait_ge(s_ys, b + 2)
                pool.wait_ge(s_ga, 16)
                gate = ga_all[:, ds(b, 1), :].broadcast_to([P, CHUNKS, D])
                g.tensor_tensor(y_sb[:, :, :], y_sb[:, :, :], gate, ALU.mult).then_inc(s_pool, 1)
                pool.wait_ge(s_pool, b + 6)
                rows = xs[:, ds(b * CHUNKS, CHUNKS), :]
                g.tensor_tensor(rows, rows, y_sb[:, :, :], ALU.add).then_inc(s_xu, 1)

            inverse_std(s_mv, CHUNKS, 1, s_rs)
            gates(1, 0)
            gates(2, 1)
            with pool.Fori(0, B - 1) as b:
                body(b, False)
            body(B - 1, True)

            with growing(pool):
                update_x(B - 1)
                g.memset(reverse[:, :], 0.0).then_inc(s_fc, 1)
                g.memset(band[:, :], 0.0).then_inc(s_fc, 1)
                pool.wait_ge(s_fc, 2)
                for h in range(2):
                    half = reverse[:, h * DK:(h + 1) * DK]
                    g.affine_select(out=half, in_=half, compare_op=ALU.not_equal, fill=1.0,
                                    base=-((h + 1) * DK - 1), pattern=[[1, DK]], channel_multiplier=1).then_inc(s_fc, 1)
                    column = (h + 1) * DK - 1
                    pool.wait_ge(s_fc, 2 * h + 3)
                    g.memset(band[h * DK:(h + 1) * DK, column:column + 1], 1.0).then_inc(s_fc, 1)
                    pool.wait_ge(s_fc, 2 * h + 4)
                with pool.Fori(0, B) as b:
                    alone(s_fmv, b + 1)
                    g.tensor_scalar(veps[:, 0:CHUNKS], mv[:, 0:CHUNKS, 1], EPS, None, ALU.add).then_inc(s_fve, 1)
                    pool.wait_ge(s_fve, b + 1)
                    g.tensor_tensor(rstd[:, 0:CHUNKS], veps[:, 0:CHUNKS], neg_half[:, 0:CHUNKS], ALU.pow).then_inc(s_frs, 1)

            def logits_exp(n):
                pool.wait_ge(s_lg, n)
                g.tensor_tensor(lg_e[:, :, :], inv_e[:, :, :], lg[:, :, :], ALU.pow).then_inc(s_le, 1)

            inverse_std(s_mv2, ST, 1, s_rs2)
            with not_growing(pool):
                update_x(B - 1)
            logits_exp(1)
            pool.wait_ge(s_gb, 16)

            def expert_step(j, last):
                for e in range(1, NE):
                    pool.wait_ge(s_cb, j * NE + e + 2)
                    if e > 1:
                        pool.wait_ge(s_add, j * E + e)
                    g.tensor_tensor(acc[:, :, :], acc[:, :, :], part[:, e % 2, :, :], ALU.add).then_inc(s_add, 1)
                    if e == 1 and not last:
                        inverse_std(s_mv2, ST, j + 2, s_rs2)
                    if e == 5 and not last:
                        logits_exp(j + 2)
                pool.wait_ge(s_add, j * E + E + 1)
                gate = gb_all[:, ds(j * (STEP // T), STEP // T), :].rearrange("p (b a) d -> p b a d", a=1).broadcast_to([P, STEP // T, CHUNKS, D])
                a4 = acc[:, :, :].rearrange("p (b a) d -> p b a d", a=CHUNKS)
                g.tensor_tensor(a4, a4, gate, ALU.mult).then_inc(s_pool, 1)
                pool.wait_ge(s_pool, j + B + 6)
                rows = xs[:, ds(j * ST, ST), :]
                g.tensor_tensor(rows, rows, acc[:, :, :], ALU.add).then_inc(s_fin, 1)

            with pool.Fori(0, STEPS - 1) as j:
                expert_step(j, False)
            expert_step(STEPS - 1, True)

        @block.scalar
        def _(sc):
            a = nc.scalar
            sc.wait_ge(s_c, 16)
            a.activation(c_e[:, :], c_in[:, :], ACT.Exp, scale=-1.0).then_inc(s_ce, 1)

            def modulate(shift, b):
                return mod[:, shift + 1, ds(b, 1)], mod[:, shift, ds(b, 1)]

            def tanh_exp(n, p, par):
                sc.wait_ge(s_z, n)
                a.activation(th[:, par, :], Z[:, 0:T], ACT.Tanh, scale=0.5, bias=half_bg[:, p:p + 1]).then_inc(s_th, 1)
                a.activation(ex[:, par, :], Z[:, 0:T], ACT.Exp, scale=-1.0, bias=neg_bg[:, p:p + 1]).then_inc(s_te, 1)

            def copy_v(n, half, chunk):
                sc.wait_ge(s_vp, n)
                a.activation(v_sb[:, chunk, half * 512:(half + 1) * 512], V[:, :], ACT.Copy).then_inc(s_v, 1)

            def h_attention(b, n):
                sc.wait_ge(s_T, n)
                scale, shift = modulate(0, b)
                a.activation(h_full[:, 0:T], M[:, 0:T], ACT.Identity, scale=scale, bias=shift).then_inc(s_hf, 1)

            def copy_o(n, p):
                sc.wait_ge(s_av, n)
                a.activation(oT[:, p, :], O[:, 0:T], ACT.Copy).then_inc(s_o, 1)

            for k, m in enumerate(W_ORDER):
                if k == 1:
                    sc.wait_ge(s_rowsT, 1)
                    a.activation(half_bg[:, :], bgT[:, :], ACT.Copy, scale=0.5)
                    a.activation(neg_bg[:, :], bgT[:, :], ACT.Copy, scale=-1.0).then_inc(s_const, 1)
                if k == 2:
                    sc.wait_ge(s_mod, 1)
                    h_attention(0, 1)
                sc.wait_ge(s_w_in[m], 16)
                a.activation(w_hi[:, m, :], w_in[:, m, :], ACT.Copy).then_inc(s_whi, 1)
            sc.wait_ge(s_const, 7)
            def body(b, last):
                for p in range(PAIRS):
                    n = b * PAIRS + p + 1
                    more = not (last and p == PAIRS - 1)
                    if more:
                        tanh_exp(n + 1, (p + 1) % PAIRS, (p + 1) % 2)
                    if p < 2:
                        copy_v(b * 4 + 3 + p, 1, p)
                    if p == 6 and not last:
                        h_attention(b + 1, b + 2)
                    if p == 7 and not last:
                        copy_v(b * 4 + 5, 0, 0)
                    sc.wait_ge(s_sx, n + 1)
                    a.activation(A[:, p % 2, :, 1, :], SX[:, 0:2 * P].rearrange("p (h t) -> p h t", h=2),
                                 ACT.Copy).then_inc(s_ax, 1)
                    if p > 0:
                        copy_o(n - 1, p - 1)
                if not last:
                    copy_v(b * 4 + 6, 0, 1)
                copy_o(b * PAIRS + PAIRS, PAIRS - 1)
                sc.wait_ge(s_y, b + 1)
                sc.wait_ge(s_xu, b + 1)
                a.activation(y_sb[:, :, :], Y[:, 0:CHUNKS * D].rearrange("p (c d) -> p c d", c=CHUNKS),
                             ACT.Copy).then_inc(s_ys, 1)

            tanh_exp(1, 0, 0)
            copy_v(1, 0, 0)
            copy_v(2, 0, 1)
            with sc.Fori(0, B - 1) as b:
                body(b, False)
            body(B - 1, True)

            with growing(sc):
                with sc.Fori(0, B) as b:
                    sc.wait_ge(s_fT, b + 1)
                    scale, shift = modulate(0, b)
                    a.activation(h_full[:, 0:T], M[:, 0:T], ACT.Identity, scale=scale, bias=shift).then_inc(s_fh, 1)
                    with sc.Fori(0, PAIRS) as p:
                        sc.wait_ge(s_fp, b * PAIRS + p + 1)
                        a.activation(seq_a, QK[1][:, 0:T], ACT.Tanh, scale=0.5, bias=half_bg[:, ds(p, 1)]).then_inc(s_fa, 1)

            def h_experts(j, n):
                sc.wait_ge(s_T2, n)
                for k in range(STEP // T):
                    scale, shift = modulate(2, j * (STEP // T) + k)
                    ins = a.activation(h_full[:, k * T:(k + 1) * T], M2[:, k * T:(k + 1) * T], ACT.Identity,
                                       scale=scale, bias=shift)
                ins.then_inc(s_hf2, 1)

            def silus(j, e):
                for i in range(IT):
                    u = j * NE * IT + e * IT + i + 1
                    sc.wait_ge(s_g, u)
                    a.activation(silu[:, i, :], GU[i][0][:, :], ACT.Silu).then_inc(s_silu, 1)

            def scale_down(j, e):
                sc.wait_ge(s_dn, j * NE + e + 1)
                bank = DN[e % 2][:, :].rearrange("p (n d) -> p n d", n=ST)
                if e == 0:
                    sc.wait_ge(s_fin, j + 1)
                    a.activation(acc[:, :, :], bank, ACT.Copy).then_inc(s_cb, 1)
                    return
                if e == 1:
                    sc.wait_ge(s_wt, j + 1)
                else:
                    sc.wait_ge(s_add, j * E + e - 1)
                for n in range(ST):
                    ins = a.activation(part[:, e % 2, n, :], bank[:, n, :], ACT.Copy, scale=wts[:, n, e - 1:e])
                ins.then_inc(s_cb, 1)

            def expert_step(j, last):
                silus(j, 0)
                for e in range(1, NE):
                    silus(j, e)
                    if e == 5 and not last:
                        h_experts(j + 1, j + 2)
                    scale_down(j, e - 1)
                scale_down(j, NE - 1)

            h_experts(0, 1)
            a.activation(table[:, :], ones[:, :], ACT.Silu)
            with sc.Fori(0, STEPS - 1) as j:
                expert_step(j, False)
            expert_step(STEPS - 1, True)

        @block.vector
        def _(dve):
            v = nc.vector
            own = [0]

            def then(ins):
                own[0] += 1
                ins.then_inc(s_dve, 1)
                dve.wait_ge(s_dve, own[0])


            def alone(semaphore, count):
                count = count if isinstance(count, int) else dve.to_reg(count)
                dve.wait_ge(s_ident, 1)
                dve.wait_ge(semaphore, count)

            def moments(tile0, n_tiles, base, signal):
                for n in range(n_tiles):
                    rows = xs[:, ds(tile0 + n, 1), :].rearrange("p a d -> p (a d)")
                    st = v.bn_stats(stats[:, n, :], rows)
                st.then_inc(s_st, 1)
                alone(s_st, base)
                for n in range(n_tiles):
                    ag = v.bn_aggr(mv[:, n, :], stats[:, n, :])
                ag.then_inc(signal, 1)

            def normalise(tile0, n_tiles, ready, count, signal):
                dve.wait_ge(ready, count)
                for n in range(n_tiles):
                    rows = xs[:, ds(tile0 + n, 1), :].rearrange("p a d -> p (a d)")
                    ins = v.tensor_scalar(xn[:, n, :], rows, mv[:, n, 0:1], rstd[:, n:n + 1], ALU.subtract, ALU.mult)
                ins.then_inc(signal, 1)

            def split_h(width, ready, count, signal):
                dve.wait_ge(ready, count)
                v.tensor_copy(h_hi[:, 0:width], h_full[:, 0:width]).then_inc(s_hh, 1)
                dve.wait_ge(s_hh, count if ready is s_hf else count + B)
                v.tensor_tensor(h_lo[:, 0:width], h_full[:, 0:width], h_hi[:, 0:width].bitcast(f32),
                                ALU.subtract).then_inc(signal, 1)

            dve.wait_ge(s_ce, 1)
            then(v.tensor_scalar(c_e[:, :], c_e[:, :], 1.0, None, ALU.add))
            then(v.reciprocal(c_s[:, :], c_e[:, :]))
            v.tensor_tensor(c_s[:, :], c_s[:, :], c_in[:, :], ALU.mult).then_inc(s_cs, 1)
            dve.wait_ge(s_cT_ps, 1)
            v.tensor_copy(cT[:, :], QK[0][:, 0:B]).then_inc(s_cT, 1)
            dve.wait_ge(s_x, 16)
            moments(0, CHUNKS, 1, s_mv)
            normalise(0, CHUNKS, s_rs, 1, s_xn)

            dve.wait_ge(s_mod_ps, 1)
            for k in range(4):
                ps = QK[1][:, k * B:(k + 1) * B]
                last = v.tensor_scalar(mod[:, k, :], ps, float(k % 2), None, ALU.add)
            last.then_inc(s_mod, 1)
            dve.wait_ge(s_rows_ps, 1)
            v.tensor_copy(bgT[:, :], SD[0][:, 0:PAIRS]).then_inc(s_rowsT, 1)
            v.tensor_copy(rwT[:, :], SD[0][:, PAIRS:PAIRS + E]).then_inc(s_rowsT, 1)

            def low_weights(k):
                m = W_ORDER[k]
                dve.wait_ge(s_whi, k + 1)
                v.tensor_tensor(w_lo[:, m, :], w_in[:, m, :], w_hi[:, m, :].bitcast(f32), ALU.subtract).then_inc(s_wsplit, 1)

            low_weights(0)
            low_weights(1)
            split_h(T, s_hf, 1, s_hl)
            low_weights(2)
            low_weights(3)
            dve.wait_ge(s_grow_ps, 1)
            gp = O[0:B, 0:2 * D].rearrange("b (k d) -> b k d", k=2)
            then(v.tensor_scalar(gsign[:, :, :], gp, 0.0, 2.0, ALU.is_ge, ALU.mult))
            then(v.tensor_scalar(grow[:, :, :], gp, -1.0, GATE_FLOOR, ALU.mult, ALU.max))
            then(v.tensor_tensor(grow[:, :, :], gp, grow[:, :, :], ALU.max))
            v.scalar_tensor_tensor(grow[:, :, :].rearrange("b k d -> b (k d)"), gsign[:, :, :].rearrange("b k d -> b (k d)"),
                                   -1.0, grow[:, :, :].rearrange("b k d -> b (k d)"), ALU.add, ALU.mult).then_inc(s_grow, 1)
            dve.wait_ge(s_sh_ps, 1)
            v.tensor_copy(shared_gu_in, SX[:, :])
            dve.wait_ge(s_sh_ps, 2)
            v.tensor_copy(down[:, 0, :, :].rearrange("p i d -> p (i d)"), O[:, 0:I]).then_inc(s_sh, 1)

            hi_flat, lo_flat = (w[:, :, :, :].rearrange("p e m n -> p (e m n)") for w in (gu_hi, gu_lo))

            def split_experts(first, raw, count):
                cols = ds(first, raw.shape[1])
                v.tensor_copy(hi_flat[:, cols], raw).then_inc(s_guhi, 1)
                dve.wait_ge(s_guhi, count)
                v.tensor_tensor(lo_flat[:, cols], raw, hi_flat[:, cols].bitcast(f32), ALU.subtract).then_inc(s_gusplit, 1)

            def products(n, par):
                dve.wait_ge(s_at, n)
                for k in range(CHUNKS):
                    cols = slice(k * P, (k + 1) * P)
                    v.tensor_tensor_scan(F[:, par, cols], ga_t[:, par, cols], ga_t[:, par, cols], 1.0, ALU.mult, ALU.min)
                dve.wait_ge(s_a, n)
                for k in range(CHUNKS):
                    cols = slice(k * P, (k + 1) * P)
                    ins = v.tensor_tensor_scan(G[:, par, cols], gi_t[:, par, cols], cap[:, :], 1.0, ALU.mult, ALU.min)
                ins.then_inc(s_fg, 1)
                dve.wait_ge(s_fg, n)
                dve.wait_ge(s_qk, n)
                v.tensor_tensor(kt[:, par, :], QK[par][:, T:2 * T], G[:, par, :], ALU.mult).then_inc(s_kt, 1)
                for h in range(2):
                    rows = slice(h * DK, (h + 1) * DK)
                    ins = v.tensor_tensor(qz[rows, par, :, h, :],
                                          QK[par][rows, 0:T].rearrange("p (c t) -> p c t", c=CHUNKS),
                                          F[rows, par, :].rearrange("p (c t) -> p c t", c=CHUNKS), ALU.mult)
                ins.then_inc(s_qt, 1)
                dve.wait_ge(s_kt, n)
                v.tensor_scalar(kx[:, par, :], kt[:, par, 0:P], F[:, par, P - 1:P], None, ALU.mult).then_inc(s_kx, 1)
                ends = G[:, par, :].rearrange("p (c t) -> p c t", c=CHUNKS)[:, :, P - 1]
                v.tensor_tensor(grown[:, :], grown[:, :], ends, ALU.max).then_inc(s_gm, 1)

            def body(b, last):
                if not last:
                    moments(b * CHUNKS + CHUNKS, CHUNKS, b + 2, s_mv)
                for p in range(PAIRS):
                    n = b * PAIRS + p + 1
                    if p == 6 and not last:
                        split_h(T, s_hf, b + 2, s_hl)
                    def next_products():
                        dve.wait_ge(s_sx, n)
                        products(n + 1, (p + 1) % 2)
                    if p < PAIRS - 1:
                        next_products()
                    alone(s_sd, n)
                    dst = A[:, p % 2, :, 0:3:2, :].rearrange("p h c t -> p c h t")
                    src = SD[p % 2][:, :].rearrange("p (c h t) -> p c h t", c=CHUNKS, h=2)
                    keep = causal[:, :].bitcast(i32).rearrange("p (a e t) -> p a e t", a=1, e=1).broadcast_to([P, CHUNKS, 2, P])
                    v.copy_predicated(dst, keep, src).then_inc(s_am, 1)
                    if p == PAIRS - 1:
                        if not last:
                            next_products()
                        dve.wait_ge(s_gu_in, 32)
                        split_experts(b * SLICE + 2 * I, gu_in[:, ds(b * SLICE, SLICE)], b + 1)
                        if last:
                            split_experts(0, shared_gu_in, B + 1)
                    if p == 4 and not last:
                        dve.wait_ge(s_x_rest, 16)
                        normalise(b * CHUNKS + CHUNKS, CHUNKS, s_rs, b + 2, s_xn)

            dve.wait_ge(s_const, 7)
            products(1, 0)
            dve.wait_ge(s_sh, 1)
            dve.wait_ge(s_x_next, 16)
            with dve.Fori(0, B - 1) as b:
                body(b, False)
            body(B - 1, True)

            dve.wait_ge(s_gm, B * PAIRS)
            v.tensor_tensor(flag_p[:, :], grown[:, 0:1], grown[:, 1:2], ALU.max).then_inc(s_gm, 1)
            dve.wait_ge(s_gm, B * PAIRS + 1)
            v.tensor_scalar(flag_p[:, :], flag_p[:, :], GROWTH_MAX, None, ALU.is_ge).then_inc(s_gflag, 1)
            dve.wait_ge(s_fps, 1)
            v.tensor_scalar(flag[:, :], Z[0:1, 0:1], 1.0, None, ALU.min).then_inc(s_flag, 1)

            with growing(dve):
                dve.wait_ge(s_xr, 16)
                dve.wait_ge(s_fc, 6)
                v.memset(kx[:, 0, :], 0.0).then_inc(s_fz, 1)
                with dve.Fori(0, B) as b:
                    for n in range(CHUNKS):
                        rows = xs[:, ds(b * CHUNKS + n, 1), :].rearrange("p a d -> p (a d)")
                        st = v.bn_stats(stats[:, n, :], rows)
                    st.then_inc(s_fst, 1)
                    alone(s_fst, b + 1)
                    for n in range(CHUNKS):
                        ag = v.bn_aggr(mv[:, n, :], stats[:, n, :])
                    ag.then_inc(s_fmv, 1)
                    normalise(b * CHUNKS, CHUNKS, s_frs, b + 1, s_fxn)
                    with dve.Fori(0, PAIRS) as p:
                        n = b * PAIRS + p + 1
                        cols = ds(p * P, P)
                        v.tensor_tensor(wst, w_hi[:, :, cols].bitcast(f32), w_lo[:, :, cols].bitcast(f32), ALU.add).then_inc(s_fw, 1)
                        dve.wait_ge(s_fp, n)
                        v.tensor_copy(seq_qk, QK[0][:, :]).then_inc(s_fq, 1)
                        dve.wait_ge(s_fa, n)
                        v.tensor_copy(seq_v, QK[1][:, T:2 * T]).then_inc(s_fq, 1)
                        v.tensor_scalar(seq_a, seq_a, 0.5, 0.5, ALU.mult, ALU.add).then_inc(s_fq, 1)
                        with dve.Fori(0, DK) as i:
                            m = (b * PAIRS + p) * DK + i + 1
                            dve.wait_ge(s_fq, n * 3)
                            dve.wait_ge(s_fo, m)
                            v.tensor_copy(spread.rearrange("k (h n) -> k h n", h=2),
                                          reverse[:, :].rearrange("k (h n) -> k h n", h=2)[:, :, ds(i, 1)].broadcast_to([P, 2, DK]))
                            v.tensor_copy(place, band[:, ds(i, P)]).then_inc(s_fs, 1)
                            dve.wait_ge(s_fb, m)
                            v.tensor_tensor(seq_kv, V[:, 0:T], seq_qk[:, T:2 * T], ALU.mult).then_inc(s_fv, 1)
                            dve.wait_ge(s_fv, m * 2 - 1)
                            v.tensor_tensor_scan(seq_S, seq_a, seq_kv, 0.0, ALU.mult, ALU.add).then_inc(s_fv, 1)
                            dve.wait_ge(s_fv, m * 2)
                            v.tensor_tensor(seq_qS, seq_S, seq_qk[:, 0:T], ALU.mult).then_inc(s_fqs, 1)
                        dve.wait_ge(s_fcl, n)
                        v.tensor_copy(seq_o[:, ds(p, 1), :].rearrange("p a t -> p (a t)"), O[:, 0:T]).then_inc(s_fot, 1)
                    dve.wait_ge(s_fy, b + 1)
                    v.tensor_tensor(y_sb[:, :, :], M[:, 0:CHUNKS * D].rearrange("p (c d) -> p c d", c=CHUNKS),
                                    ga_all[:, ds(b, 1), :].broadcast_to([P, CHUNKS, D]), ALU.mult).then_inc(s_fyg, 1)
                    dve.wait_ge(s_fyg, b + 1)
                    rows = xs[:, ds(b * CHUNKS, CHUNKS), :]
                    v.tensor_tensor(rows, rows, y_sb[:, :, :], ALU.add).then_inc(s_fx, 1)
                dve.wait_ge(s_fx, B)

            dve.wait_ge(s_xu, 3)
            moments(0, ST, B + 1, s_mv2)
            normalise(0, ST, s_rs2, 1, s_xn2)
            split_h(STEP, s_hf2, 1, s_hl2)

            def gate_times_up(j, e, i):
                u = j * NE * IT + e * IT + i + 1
                dve.wait_ge(s_silu, u)
                dve.wait_ge(s_u, u)
                v.tensor_tensor(act[:, e % 2, i, :], GU[i][1][:, :], silu[:, i, :], ALU.mult).then_inc(s_act, 1)

            def logits(n):
                dve.wait_ge(s_r, n)
                v.tensor_tensor(lg[:, :, :], R[:, 0:ST * E].rearrange("p (n e) -> p n e", n=ST),
                                rbias[:, :].rearrange("p (a e) -> p a e", a=1).broadcast_to([P, ST, E]), ALU.add).then_inc(s_lg, 1)

            def routed(j, count):
                alone(s_rt, j * 8 + count)

            def route_sigmoid(j):
                dve.wait_ge(s_le, j + 1)
                v.tensor_scalar(lg_1[:, :, :], lg_e[:, :, :], 1.0, 1.0, ALU.mult, ALU.add).then_inc(s_rt, 1)
                routed(j, 1)
                v.reciprocal(pr[:, :, :], lg_1[:, :, :]).then_inc(s_rt, 1)
                routed(j, 2)
                for n in range(ST):
                    ins = v.max(top[:, n, :], pr[:, n, :])
                ins.then_inc(s_rt, 1)

            def route_choice(j):
                routed(j, 3)
                for n in range(ST):
                    ins = v.max_index(top_i[:, n, :], top[:, n, :], pr[:, n, :])
                v.tensor_tensor(tsum[:, :], top[:, :, 0], top[:, :, 1], ALU.add).then_inc(s_rt, 1)

            def route_scores(j):
                routed(j, 4)
                v.tensor_copy(top_f[:, :, :], top_i[:, :, 0:TOP])
                v.reciprocal(trec[:, :], tsum[:, :]).then_inc(s_rt, 1)
                routed(j, 5)
                for t in range(TOP):
                    v.tensor_tensor(pick[:, t, :, :], iota8[:, :].rearrange("p (a e) -> p a e", a=1).broadcast_to([P, ST, E]),
                                    top_f[:, :, t:t + 1].broadcast_to([P, ST, E]), ALU.is_equal)
                v.tensor_tensor(score[:, :, :], top[:, :, 0:TOP],
                                trec[:, :].rearrange("p (n a) -> p n a", a=1).broadcast_to([P, ST, TOP]), ALU.mult).then_inc(s_rt, 1)

            def route_weights(j):
                routed(j, 6)
                for t in range(TOP):
                    ins = v.tensor_tensor(pick[:, t, :, :], pick[:, t, :, :],
                                          score[:, :, t:t + 1].broadcast_to([P, ST, E]), ALU.mult)
                    ins.then_inc(s_rt, 1)
                routed(j, 8)
                dve.wait_ge(s_cb, j * NE + 1)
                v.tensor_tensor(wts[:, :, :], pick[:, 0, :, :], pick[:, 1, :, :], ALU.add).then_inc(s_wt, 1)

            routing = {(0, 1): route_sigmoid, (1, 0): route_choice, (1, 1): route_scores, (2, 0): route_weights}
            dve.wait_ge(s_misc, 32)
            logits(1)

            def expert_step(j, last):
                for e in range(NE):
                    for i in range(IT):
                        gate_times_up(j, e, i)
                        if (e, i) in routing:
                            routing[e, i](j)
                    if last:
                        continue
                    if e == 1:
                        moments(j * ST + ST, ST, j + B + 2, s_mv2)
                    if e == 3:
                        normalise(j * ST + ST, ST, s_rs2, j + 2, s_xn2)
                    if e == 6:
                        logits(j + 2)
                    if e == NE - 1:
                        split_h(STEP, s_hf2, j + 2, s_hl2)

            with dve.Fori(0, STEPS - 1) as j:
                expert_step(j, False)
            expert_step(STEPS - 1, True)

        @block.tensor
        def _(pe):
            t = nc.tensor

            def transpose(dst, src, n):
                return t.transpose(dst, src, ident[0:n, 0:n])

            def three_passes(dst, hi, lo, m_hi, m_lo):
                t.matmul(dst, hi, m_hi, start=True, stop=False)
                t.matmul(dst, hi, m_lo, start=False, stop=False)
                return t.matmul(dst, lo, m_hi, start=False, stop=True)

            wmod_sb = gb_all[:, 0:6, :]
            pe.wait_ge(s_ident, 1)
            pe.wait_ge(s_cs, 1)
            transpose(QK[0][:, 0:B], c_s[:, :], B).then_inc(s_cT_ps, 1)
            pe.wait_ge(s_cT, 1)
            pe.wait_ge(s_wmod, 16)
            for k, m in enumerate((0, 1, 3, 4)):
                last = t.matmul(QK[1][:, k * B:(k + 1) * B], wmod_sb[:, m, :], cT[:, :], start=True, stop=True)
            last.then_inc(s_mod_ps, 1)
            for k, m in enumerate((2, 5)):
                last = t.matmul(O[0:B, k * D:(k + 1) * D], cT[:, :], wmod_sb[:, m, :], start=True, stop=True)
            last.then_inc(s_grow_ps, 1)
            pe.wait_ge(s_rows, 32)
            transpose(SD[0][:, 0:PAIRS], rows8[:, 0, :], E)
            transpose(SD[0][:, PAIRS:PAIRS + E], rows8[:, 1, :], E).then_inc(s_rows_ps, 1)
            def xn_transposed(bank, n_tiles, ready, count, signal):
                pe.wait_ge(ready, count)
                for n in range(n_tiles):
                    last = transpose(bank[:, n * P:(n + 1) * P], xn[:, n, :], P)
                last.then_inc(signal, 1)

            def project_z(p):
                cols = slice(p * P, (p + 1) * P)
                three_passes(Z[:, 0:T], w_hi[:, 2, cols], w_lo[:, 2, cols], h_hi[:, 0:T], h_lo[:, 0:T]).then_inc(s_z, 1)

            def project_qk(p, par):
                cols = slice(p * P, (p + 1) * P)
                for m, off in ((0, 0), (1, T)):
                    last = three_passes(QK[par][:, off:off + T], w_hi[:, m, cols], w_lo[:, m, cols], h_hi[:, 0:T], h_lo[:, 0:T])
                last.then_inc(s_qk, 1)

            def values(half, chunk):
                cols, rows = slice(half * 512, (half + 1) * 512), slice(chunk * P, (chunk + 1) * P)
                t.matmul(V[:, :], h_hi[:, rows], w_hi[:, 3, cols], start=True, stop=False)
                t.matmul(V[:, :], h_hi[:, rows], w_lo[:, 3, cols], start=False, stop=False)
                t.matmul(V[:, :], h_lo[:, rows], w_hi[:, 3, cols], start=False, stop=True).then_inc(s_vp, 1)

            def scores(n, par):
                pe.wait_ge(s_kt, n)
                pe.wait_ge(s_qt, n)
                for k in range(CHUNKS):
                    last = t.matmul(SD[par][:, k * 2 * P:(k + 1) * 2 * P], kt[:, par, k * P:(k + 1) * P],
                                    qz[:, par, k, :, :].rearrange("p h t -> p (h t)"), start=True, stop=True)
                last.then_inc(s_sd, 1)
                pe.wait_ge(s_kx, n)
                pe.wait_ge(s_ax, n)
                t.matmul(SX[:, 0:2 * P], kx[:, par, :], qz[:, par, 1, :, :].rearrange("p h t -> p (h t)"),
                         start=True, stop=True).then_inc(s_sx, 1)

            def attend(n, p, par):
                pe.wait_ge(s_am, n + 1)
                pe.wait_ge(s_ax, n + 1)
                pe.wait_ge(s_o, n)
                for k in range(CHUNKS):
                    for h in range(2):
                        vcols = slice((2 * p + h) * DK, (2 * p + h + 1) * DK)
                        blocks = A[:, par, h, 0:2, :] if k == 0 else A[:, par, h, 2:3, :]
                        last = t.matmul(O[h * DK:(h + 1) * DK, k * P:T], v_sb[:, k, vcols],
                                        blocks.rearrange("p c t -> p (c t)"), start=(k == 0), stop=(k == CHUNKS - 1))
                last.then_inc(s_av, 1)

            def output(b):
                for k in range(CHUNKS):
                    for p in range(PAIRS):
                        if k == 0 and p == PAIRS - 1:
                            pe.wait_ge(s_o, b * PAIRS + PAIRS + 1)
                        last = t.matmul(Y[:, k * D:(k + 1) * D], oT[:, p, k * P:(k + 1) * P], wo[:, p, :],
                                        start=(p == 0), stop=(p == PAIRS - 1))
                last.then_inc(s_y, 1)

            def body(b, last):
                for p in range(PAIRS):
                    n = b * PAIRS + p + 1
                    if not (last and p == PAIRS - 1):
                        pe.wait_ge(s_te, n)
                        if p == PAIRS - 1:
                            pe.wait_ge(s_hl, b + 2)
                        project_z((p + 1) % PAIRS)
                        project_qk((p + 1) % PAIRS, (p + 1) % 2)
                    if p < 2:
                        pe.wait_ge(s_v, b * 4 + 2 + p)
                        values(1, p)
                    if p == 6 and not last:
                        xn_transposed(M, CHUNKS, s_xn, b + 2, s_T)
                    if p == 7 and not last:
                        pe.wait_ge(s_v, b * 4 + 4)
                        values(0, 0)
                    if p == 0:
                        pe.wait_ge(s_ys, b + 1)
                    scores(n, p % 2)
                    if p > 0:
                        if p == 1:
                            pe.wait_ge(s_v, b * 4 + 2)
                        if p == 5:
                            pe.wait_ge(s_v, b * 4 + 4)
                        attend(n - 1, p - 1, (p - 1) % 2)
                if not last:
                    pe.wait_ge(s_v, b * 4 + 5)
                    values(0, 1)
                attend(b * PAIRS + PAIRS, PAIRS - 1, 1)
                if last:
                    pe.wait_ge(s_gflag, 1)
                    t.matmul(Z[0:1, 0:1], flag_p[:, :], ones[:, :], start=True, stop=True).then_inc(s_fps, 1)
                output(b)

            xn_transposed(M, CHUNKS, s_xn, 1, s_T)
            pe.wait_ge(s_hl, 1)
            pe.wait_ge(s_wsplit, 1)
            project_z(0)
            pe.wait_ge(s_wsplit, 3)
            project_qk(0, 0)
            pe.wait_ge(s_wsplit, 4)
            values(0, 0)
            pe.wait_ge(s_sh_in, 48)
            for m in range(2):
                for i in range(IT):
                    last = transpose(SX[:, (m * IT + i) * P:(m * IT + i + 1) * P], ga_all[:, m * IT + i, :], P)
            last.then_inc(s_sh_ps, 1)
            pe.wait_ge(s_grow, 1)
            for i in range(IT):
                last = transpose(O[:, i * P:(i + 1) * P], ga_all[:, 4 + i, :], P)
            last.then_inc(s_sh_ps, 2)

            pe.wait_ge(s_v, 1)
            values(0, 1)
            pe.wait_ge(s_wo, 16)
            pe.wait_ge(s_sh, 1)
            with pe.Fori(0, B - 1) as b:
                body(b, False)
            body(B - 1, True)

            with growing(pe):
                pe.wait_ge(s_fz, 1)
                with pe.Fori(0, B) as b:
                    xn_transposed(M, CHUNKS, s_fxn, b + 1, s_fT)
                    with pe.Fori(0, PAIRS) as p:
                        n = b * PAIRS + p + 1
                        pe.wait_ge(s_fh, b + 1)
                        pe.wait_ge(s_fw, n)
                        for m, dst in enumerate((QK[0][:, 0:T], QK[0][:, T:2 * T], QK[1][:, 0:T], QK[1][:, T:2 * T])):
                            last = t.matmul(dst, wst[:, m, :], h_full[:, 0:T], start=True, stop=True)
                        last.then_inc(s_fp, 1)
                        pe.wait_ge(s_fq, n * 3)
                        t.matmul(O[:, 0:T], kx[:, 0, :], seq_v, start=True, stop=False)
                        with pe.Fori(0, DK) as i:
                            m = (b * PAIRS + p) * DK + i + 1
                            pe.wait_ge(s_fs, m)
                            t.matmul(V[:, 0:T], spread, seq_v, start=True, stop=True).then_inc(s_fb, 1)
                            pe.wait_ge(s_fqs, m)
                            t.matmul(O[:, 0:T], place, seq_qS, start=False, stop=False).then_inc(s_fo, 1)
                        t.matmul(O[:, 0:T], kx[:, 0, :], seq_v, start=False, stop=True).then_inc(s_fcl, 1)
                    pe.wait_ge(s_fot, b * PAIRS + PAIRS)
                    for k in range(CHUNKS):
                        for p in range(PAIRS):
                            last = t.matmul(M[:, k * D:(k + 1) * D], seq_o[:, p, k * P:(k + 1) * P], wo[:, p, :],
                                            start=(p == 0), stop=(p == PAIRS - 1))
                    last.then_inc(s_fy, 1)

            pe.wait_ge(s_gusplit, B + 1)
            pe.wait_ge(s_misc, 32)

            def router(n):
                pe.wait_ge(s_hf2, n)
                for k in range(ST):
                    ins = t.matmul(R[:, k * E:(k + 1) * E], h_full[:, k * P:(k + 1) * P], rwT[:, :], start=True, stop=True)
                ins.then_inc(s_r, 1)

            xn_transposed(M2, ST, s_xn2, 1, s_T2)
            pe.wait_ge(s_ys, B + 1)
            router(1)

            def gate_up(j, e):
                for i in range(IT):
                    u = j * NE * IT + e * IT + i + 1
                    cols = slice(i * P, (i + 1) * P)
                    if e > 0:
                        pe.wait_ge(s_act, u - 2)
                    for m, signal in ((0, s_g), (1, s_u)):
                        three_passes(GU[i][m][:, :], gu_hi[:, e, m, cols], gu_lo[:, e, m, cols],
                                     h_hi[:, :], h_lo[:, :]).then_inc(signal, 1)

            def down_project(j, e):
                pe.wait_ge(s_act, j * NE * IT + (e + 1) * IT)
                pe.wait_ge(s_cb, j * NE + max(e - 1, 0) + 1)
                for n in range(ST):
                    for i in range(IT):
                        last = t.matmul(DN[e % 2][:, n * D:(n + 1) * D], act[:, e % 2, i, n * P:(n + 1) * P],
                                        down[:, e, i, :], start=(i == 0), stop=(i == IT - 1))
                last.then_inc(s_dn, 1)

            def expert_step(j, last):
                pe.wait_ge(s_hl2, j + 1)
                gate_up(j, 0)
                for e in range(1, NE):
                    gate_up(j, e)
                    down_project(j, e - 1)
                    if e == 4 and not last:
                        xn_transposed(M2, ST, s_xn2, j + 2, s_T2)
                    if e == 6 and not last:
                        router(j + 2)
                down_project(j, NE - 1)

            with pe.Fori(0, STEPS - 1) as j:
                expert_step(j, False)
            expert_step(STEPS - 1, True)


_INS = ['L0_attn_x', 'L0_attn_W_q', 'L0_attn_W_k', 'L0_attn_W_v', 'L0_attn_W_gate', 'L0_attn_b_gate', 'L0_attn_W_o',
        'L0_ffn_shared_gate', 'L0_ffn_shared_up', 'L0_ffn_shared_down', 'L0_ffn_gate_w', 'L0_ffn_up_w',
        'L0_ffn_down_w', 'L0_ffn_router_w', 'L0_ffn_routing_bias', 'L0_c', 'L0_wmod']


def kernel(**inputs):
    import numpy as _np
    import concourse.bacc as _bacc
    from concourse.bass_utils import run_bass_kernel_spmd as _run

    nc = _bacc.Bacc("TRN2", target_bir_lowering=False, num_devices=1)
    arrays, args = {}, []
    for name in _INS:
        a = _np.ascontiguousarray(inputs[name])
        arrays[f"in_{name}_dram"] = a
        args.append(nc.dram_tensor(f"in_{name}_dram", a.shape, mybir.dt.from_np(a.dtype), kind="ExternalInput").ap())
    args.append(nc.dram_tensor("out_0_dram", (B, T, D), mybir.dt.float32, kind="ExternalOutput").ap())
    block_kernel(nc, *args)
    r = _run(nc, [arrays], core_ids=[0])
    return r.results[0]["out_0_dram"]
```
